# Optimizing a Trainium2 kernel written in Bass

```python
import numpy as np
import jax
import jax.numpy as jnp

def _softmax(x, axis=-1):
    return jax.nn.softmax(x, axis=axis)

def _gelu(x):
    return jax.nn.gelu(x, approximate=True)

def _silu(x):
    return jax.nn.silu(x)

def _sigmoid(x):
    return jax.nn.sigmoid(x)

def _layernorm(x, axis=-1, eps=1e-05):
    m = jnp.mean(x, axis=axis, keepdims=True)
    v = jnp.var(x, axis=axis, keepdims=True)
    return (x - m) / jnp.sqrt(v + eps)

def _scatter_add(tgt, idx, src, axis=0):
    return tgt.at[idx].add(src)

def _segment_sum(src, seg, n):
    return jax.ops.segment_sum(src, seg, n)
kernel_name = 'mk_prb_d1_jaxref_r8_0222c1'

def setup_inputs(seed: int=0):
    np.random.seed(seed)
    _w = jnp.asarray

    def _L0_attn_setup():
        import jax, jax.numpy as jnp
        import numpy as np
        D_MODEL = 256
        N_HEADS = 16
        HEAD_DIM = D_MODEL // N_HEADS
        NEG_BIG = -1e+30
        key = jax.random.key(seed)
        ks = jax.random.split(key, 9)
        B, T = (2, 256)
        s_in = 1.0 / np.sqrt(D_MODEL)
        s_hd = 1.0 / np.sqrt(D_MODEL)
        return {'q_input': jax.random.normal(ks[0], (B, T, D_MODEL), dtype=jnp.float32), 'Wq': jax.random.normal(ks[1], (D_MODEL, D_MODEL), dtype=jnp.float32) * s_in, 'bq': jnp.zeros((D_MODEL,), dtype=jnp.float32), 'Wk': jax.random.normal(ks[2], (HEAD_DIM, D_MODEL), dtype=jnp.float32) * s_in, 'bk': jnp.zeros((HEAD_DIM,), dtype=jnp.float32), 'Wv': jax.random.normal(ks[3], (HEAD_DIM, D_MODEL), dtype=jnp.float32) * s_in, 'bv': jnp.zeros((HEAD_DIM,), dtype=jnp.float32), 'Wo': jax.random.normal(ks[4], (D_MODEL, D_MODEL), dtype=jnp.float32) * s_hd, 'bo': jnp.zeros((D_MODEL,), dtype=jnp.float32)}
    _L0_attn_in = _L0_attn_setup()

    def _L0_ffn_setup():
        import jax, jax.numpy as jnp
        import numpy as np
        H = 256
        M = 176
        E = 32
        TOPK = 6
        G = 8
        TOPK_G = 4
        SH = 2
        B, S = (1, 128)
        key = jax.random.key(seed)
        ks = jax.random.split(key, 9)
        sc = 0.02
        return {'x': jax.random.normal(ks[0], (B, S, H), dtype=jnp.float32), 'w_router': jax.random.normal(ks[1], (H, E), dtype=jnp.float32) * sc, 'corr_bias': jax.random.normal(ks[2], (E,), dtype=jnp.float32) * 0.1, 'gate_w': jax.random.normal(ks[3], (E, H, M), dtype=jnp.float32) * sc, 'up_w': jax.random.normal(ks[4], (E, H, M), dtype=jnp.float32) * sc, 'down_w': jax.random.normal(ks[5], (E, M, H), dtype=jnp.float32) * sc, 'sh_gate_w': jax.random.normal(ks[6], (H, M * SH), dtype=jnp.float32) * sc, 'sh_up_w': jax.random.normal(ks[7], (H, M * SH), dtype=jnp.float32) * sc, 'sh_down_w': jax.random.normal(ks[8], (M * SH, H), dtype=jnp.float32) * sc}
    _L0_ffn_in = _L0_ffn_setup()
    _d = {'L0_attn_q_input': _L0_attn_in['q_input'], 'L0_attn_Wq': _L0_attn_in['Wq'], 'L0_attn_bq': _L0_attn_in['bq'], 'L0_attn_Wk': _L0_attn_in['Wk'], 'L0_attn_bk': _L0_attn_in['bk'], 'L0_attn_Wv': _L0_attn_in['Wv'], 'L0_attn_bv': _L0_attn_in['bv'], 'L0_attn_Wo': _L0_attn_in['Wo'], 'L0_attn_bo': _L0_attn_in['bo'], 'L0_ffn_w_router': _L0_ffn_in['w_router'], 'L0_ffn_corr_bias': _L0_ffn_in['corr_bias'], 'L0_ffn_gate_w': _L0_ffn_in['gate_w'], 'L0_ffn_up_w': _L0_ffn_in['up_w'], 'L0_ffn_down_w': _L0_ffn_in['down_w'], 'L0_ffn_sh_gate_w': _L0_ffn_in['sh_gate_w'], 'L0_ffn_sh_up_w': _L0_ffn_in['sh_up_w'], 'L0_ffn_sh_down_w': _L0_ffn_in['sh_down_w']}
    _x0 = _d['L0_attn_q_input']
    _d['L0_attn_q_input'] = jax.random.normal(jax.random.fold_in(jax.random.key(seed), 1), (4, 512, 256), dtype=_x0.dtype)
    del _x0
    return _d

def reference(L0_attn_q_input, L0_attn_Wq, L0_attn_bq, L0_attn_Wk, L0_attn_bk, L0_attn_Wv, L0_attn_bv, L0_attn_Wo, L0_attn_bo, L0_ffn_w_router, L0_ffn_corr_bias, L0_ffn_gate_w, L0_ffn_up_w, L0_ffn_down_w, L0_ffn_sh_gate_w, L0_ffn_sh_up_w, L0_ffn_sh_down_w):

    def _L0_attn_ref(q_input, Wq, bq, Wk, bk, Wv, bv, Wo, bo):
        import jax, jax.numpy as jnp
        import numpy as np
        D_MODEL = 256
        N_HEADS = 16
        HEAD_DIM = D_MODEL // N_HEADS
        NEG_BIG = -1e+30
        B, T, _ = q_input.shape
        scale = 1.0 / np.sqrt(HEAD_DIM)
        q = (q_input @ Wq.T + bq).reshape(B, T, N_HEADS, HEAD_DIM).transpose(0, 2, 1, 3)
        k = q_input @ Wk.T + bk
        v = q_input @ Wv.T + bv
        pos = jnp.arange(T)
        mask = pos[None, :] < pos[:, None]
        scores = jnp.einsum('bhtd,bsd->bhts', q, k) * scale
        scores = jnp.where(mask[None, None, :, :], scores, NEG_BIG)
        attn = jax.nn.softmax(scores, axis=-1)
        row_valid = jnp.any(mask, axis=-1)
        attn = attn * row_valid[None, None, :, None].astype(attn.dtype)
        out = jnp.einsum('bhts,bsd->bhtd', attn, v)
        out = out.transpose(0, 2, 1, 3).reshape(B, T, D_MODEL)
        out = out @ Wo.T + bo
        return out

    def _L0_ffn_ref(x, w_router, corr_bias, gate_w, up_w, down_w, sh_gate_w, sh_up_w, sh_down_w):
        import jax, jax.numpy as jnp
        import numpy as np
        H = 256
        M = 176
        E = 32
        TOPK = 6
        G = 8
        TOPK_G = 4
        SH = 2
        B, S = (1, 128)
        b, s, h = x.shape
        xf = x.reshape(-1, h)
        T = xf.shape[0]
        logits = xf @ w_router
        scores = jax.nn.sigmoid(logits)
        sfc = scores + corr_bias
        grp = sfc.reshape(T, G, E // G)
        top2, _ = jax.lax.top_k(grp, 2)
        group_scores = top2.sum(-1)
        _, gidx = jax.lax.top_k(group_scores, TOPK_G)
        group_mask = jax.nn.one_hot(gidx, G, dtype=jnp.float32).sum(axis=1) > 0
        score_mask = jnp.repeat(group_mask, E // G, axis=1)
        masked = jnp.where(score_mask, sfc, -jnp.inf)
        _, topk_idx = jax.lax.top_k(masked, TOPK)
        topk_w = jnp.take_along_axis(scores, topk_idx, axis=1)
        combine = jnp.zeros((T, E), dtype=x.dtype).at[jnp.arange(T)[:, None], topk_idx].add(topk_w)
        g = jnp.einsum('th,ehm->etm', xf, gate_w)
        u = jnp.einsum('th,ehm->etm', xf, up_w)
        eo = jnp.einsum('etm,emh->eth', jax.nn.silu(g) * u, down_w)
        routed = jnp.einsum('te,eth->th', combine, eo)
        shared = jax.nn.silu(xf @ sh_gate_w) * (xf @ sh_up_w) @ sh_down_w
        return (routed + shared).reshape(b, s, h)
    x = L0_attn_q_input
    xn = _layernorm(x, axis=-1)
    x = x + _L0_attn_ref(xn, L0_attn_Wq, L0_attn_bq, L0_attn_Wk, L0_attn_bk, L0_attn_Wv, L0_attn_bv, L0_attn_Wo, L0_attn_bo) + _L0_ffn_ref(xn, L0_ffn_w_router, L0_ffn_corr_bias, L0_ffn_gate_w, L0_ffn_up_w, L0_ffn_down_w, L0_ffn_sh_gate_w, L0_ffn_sh_up_w, L0_ffn_sh_down_w)
    return x

_drawn_inputs = setup_inputs


def setup_inputs(seed=0):
    import zlib

    import numpy as np

    out = dict(_drawn_inputs(seed))
    spreads = {'L0_attn_bq': (0.0, 0.594),
     'L0_attn_bk': (0.0, 0.8),
     'L0_attn_bv': (0.0, 0.1),
     'L0_attn_bo': (0.0, 0.1)}
    factors = {'L0_ffn_w_router': 4.273,
     'L0_ffn_corr_bias': 3.63,
     'L0_ffn_gate_w': 3.04,
     'L0_ffn_up_w': 3.011,
     'L0_ffn_down_w': 3.015,
     'L0_ffn_sh_gate_w': 2.975,
     'L0_ffn_sh_up_w': 2.924,
     'L0_ffn_sh_down_w': 2.929}
    for name, (base, spread) in spreads.items():
        noise = np.random.default_rng([zlib.crc32(name.encode()), seed]).standard_normal(out[name].shape)
        drawn = base * np.exp(spread * noise) if base else spread * noise
        out[name] = jnp.asarray(drawn.astype(out[name].dtype))
    for name, factor in factors.items():
        out[name] = (out[name] * factor).astype(out[name].dtype)
    return out
```

```python
from contextlib import ExitStack

import numpy as np

import concourse.bass as bass
from concourse import mybir

F32 = mybir.dt.float32
BF16 = mybir.dt.bfloat16
F16 = mybir.dt.float16
U32 = mybir.dt.uint32
I32 = mybir.dt.int32
ALU = mybir.AluOpType
ACT = mybir.ActivationFunctionType
AX = mybir.AxisListType.X

P = 128
B, T, D = 4, 512, 256
NTOK = B * T
NT = NTOK // P
IT = T // P
KC = D // P
NH, HD = 16, 16
E, M = 32, 176
MC = M // 2
G, GE = 8, 4
TOPK = 6
EARLY = 3
MID = EARLY + 4
PIECES = 6
K0 = 64
VRK = K0 + HD
LEAD = 8
LAST = 3
NPB = 3
NHB, NOB = 5, 9
WCOL = KC * 2 * M + 2 * D
GU = KC * 2 * M
NSLOT = (NTOK * TOPK) // P + E - 1
ROW = D + E
HUGE = 3e38
BIG = 1e30
EPS = 1e-5
SCALE = 0.25
ST_GROUP = 4


class Stream:

    def __init__(self, sem):
        self.sem, self.count, self.ops, self.seen = sem, 0, [], {}

    def __call__(self, op, after=(), signal=True):
        waits = []
        for token in after:
            if token is None:
                continue
            sem, value = token
            if self.seen.get(id(sem), 0) < value:
                self.seen[id(sem)] = value
                waits.append((sem, value))
        if signal:
            self.count += 1
        self.ops.append((waits, op, (self.sem, 1) if signal else None))
        return (self.sem, self.count) if signal else None

    def dma(self, op, sem, after=()):
        self(op, after, signal=False)
        sem[1] += 16
        self.ops[-1] = (self.ops[-1][0], op, (sem[0], 16))
        return (sem[0], sem[1])

    def wait(self, after):
        self(None, after, signal=False)

    def play(self, eng):
        for waits, op, inc in self.ops:
            for sem, value in waits:
                eng.wait_ge(sem, value)
            if op is not None:
                ins = op(eng)
                if inc:
                    ins.then_inc(*inc)


def build(nc, x, first, proj, tables, iota, shared, sdn, wts, out):
    ctx = ExitStack()
    with ctx:
        def sb(name, shape, dt=F32):
            return ctx.enter_context(nc.sbuf_tensor(name, shape, dt))

        def dsem(name):
            return [ctx.enter_context(nc.semaphore(name)), 0]

        weights = sb("weights", [P, E * WCOL])
        top = [EARLY * WCOL]

        def carve(shape, dt=F32, parts=P):
            n = int(np.prod(shape))
            words = (n * mybir.dt.size(dt) + 31) // 32 * 8
            v = weights[0:parts, top[0]:top[0] + words]
            top[0] += words
            if dt != F32:
                v = v.bitcast(dt)
            v = v[:, 0:n]
            names = "abcd"[:len(shape)]
            if len(shape) > 1:
                v = v.rearrange(f"p ({' '.join(names)}) -> p {' '.join(names)}",
                                **dict(zip(names, shape)))
            return v

        xnT = sb("xnT", [P, KC, NTOK])
        attT = sb("attT", [P, KC, NTOK])

        def parted(whole, shapes):
            at, views = 0, []
            for shape in shapes:
                n = int(np.prod(shape))
                v = whole[:, at:at + n]
                views.append(v.rearrange("p (a b) -> p a b", b=shape[-1]) if len(shape) > 1 else v)
                at += n
            assert at == whole.shape[1]
            return views

        first_sb = sb("first_sb", [P, P + 4])
        id_sb, col_sb = parted(first_sb, ((P,), (4,)))
        shared_sb = sb("shared_sb", [P, D + KC * D + KC * 4 * M])
        bo_sb, wo_sb, sgu_sb = parted(shared_sb, ((D,), (KC, D), (KC, 4 * M)))
        sdn_sb = sb("sdn_sb", [MC, 4, D])
        sh_act = sb("sh_act", [MC, 2, T])
        gidx = sb("gidx", [P, P], U32)
        sidx = sb("sidx", [P, P], U32)
        erow = sb("erow", [1, P], I32)
        tables_sb = carve([E * NT + E * E + 5 * P])
        jc_sb, ltri_sb, masks32 = parted(tables_sb, ((E, NT), (E, E), (5, P)))
        stats = carve([NT, 6])
        mv = carve([NT, 2])
        rstd = carve([NT])
        var = carve([NT])
        scores = carve([NT, E])
        sfc = carve([NT, E + 2])
        pairs = carve([2, NT, G])
        gsum = carve([NT, G + 4])
        top8 = carve([NT, 8])
        gsel = carve([NT, G + 4])
        masked = carve([NT, E + 2])
        picked = carve([NT, E + 2])
        sel = carve([NT, E])
        selb = carve([NT, E], BF16)
        comb = carve([NT, E])
        cnt = carve([E])
        cmp_a = carve([E, E])
        ntile = carve([E])
        ends = carve([E])
        offs = carve([E])
        pos = carve([NT, E])
        pos8 = carve([NT, 8])
        posu = carve([NT, 8], U32)
        hiu = carve([NT, 8], U32)
        lou = carve([NT, 8], U32)
        ecmp = carve([E])
        ecol = carve([2])
        assert top[0] >= MID * WCOL
        mask_sb = carve([5, P], BF16)
        iota_sb = carve([P], F16)
        zero_sb = carve([D])
        proj_sb = carve([KC * D + KC * VRK + KC + 1 + HD + E])
        wq_sb, wvrk_sb, bq_sb, bk_sb, bv_sb, cb_sb = parted(
            proj_sb, ((KC, D), (KC, VRK), (KC,), (1,), (HD,), (E,)))
        vr_sb = carve([2, T])
        table = carve([P])
        tokid = carve([NT])
        tabm = carve([2, P])
        hi = carve([NT, 8])
        lo = carve([NT, 8])
        NOH = IT * TOPK
        oh = carve([NOH, 2, P], F16)
        v_sb = carve([NT, 2 * HD])
        q32 = carve([NPB, T])
        parts_sb = carve([NPB, 3, T], BF16)
        qs = [carve([NH, T], BF16) for _ in range(2)]
        ks = [carve([T], BF16) for _ in range(2)]
        mx = carve([2, NH, IT])
        mrow = carve([3, P])
        mpart = carve([2, 3, P], BF16)
        lrec = carve([2, IT, ST_GROUP])
        xin = carve([NT, D])
        xin_flat = xin.rearrange("p t d -> p (t d)")
        pexp = [xin_flat[:, i * 2 * T:(i + 1) * 2 * T].rearrange("p (a b) -> p a b", a=2) for i in range(4)]
        NXN = 8
        xn = carve([NXN, D])
        o_sb = xn[:, 0:4, :].rearrange("p (a b) d -> p a (b d)", a=2)
        att = xn[:, 4:8, :]
        assert top[0] <= E * WCOL, top[0] - E * WCOL
        top[0] = EARLY * WCOL
        hidden = [carve([T]) for _ in range(NHB)]
        ores = [carve([D]) for _ in range(NOB)]
        assert top[0] <= MID * WCOL
        last_hidden = [attT[:, 1, 0:T], attT[:, 1, T:2 * T], attT[:, 1, 2 * T:3 * T], attT[:, 0, 0:T]]
        last_ores = [attT[:, 0, T + i * D:T + (i + 1) * D] for i in range(IT)]

        slot_at = [0]
        xflat = xnT[:, :, :].rearrange("p a b -> p (a b)")

        def slot_view(n):
            v = xflat[:, slot_at[0]:slot_at[0] + n]
            slot_at[0] += n
            return v

        NXG = 8
        xg = [slot_view(ROW) for _ in range(NXG)]
        xgT = [slot_view(D).rearrange("p (a b) -> p a b", a=KC) for _ in range(2)]
        sg = [slot_view(M) for _ in range(2)]
        hh = [slot_view(M) for _ in range(2)]
        hT = [slot_view(2 * P).rearrange("p (a b) -> p a b", a=2) for _ in range(2)]
        NY = 6
        ys = [attT[:, 0, D * i:D * i + D] for i in range(NY)]
        assert slot_at[0] <= KC * NTOK

        bank = ctx.enter_context(nc.psum_tensor("bank", [P, 8, 512], F32))

        rows_d = nc.dram_tensor("rows_d", [NTOK, ROW], F32).ap()
        q_d = nc.dram_tensor("q_d", [B, 3, D, T], BF16).ap()
        k_d = nc.dram_tensor("k_d", [B, 3, HD, T], BF16).ap()
        acc_d = [nc.dram_tensor(f"acc_d{i}", [NTOK + P, D], F32).ap() for i in range(2)]

        sems = {n: ctx.enter_context(nc.semaphore(n)) for n in ("pe_s", "act_s", "dve_s", "pool_s", "sp_s")}
        pe, act, dve, pool, sp = (Stream(sems[n]) for n in ("pe_s", "act_s", "dve_s", "pool_s", "sp_s"))

        x_v = x.rearrange("(t p) d -> p t d", p=P)
        x_in = [None] * (NT // 2)
        for n, (t0, t1) in enumerate(((0, 2), (2, 4), (4, 8), (8, 12), (12, 16))):
            landed = sp.dma(lambda e, t0=t0, t1=t1: e.dma_start(xin[:, t0:t1, :], x_v[:, t0:t1, :]), dsem(f"x_s{n}"))
            x_in[t0 // 2:t1 // 2] = [landed] * ((t1 - t0) // 2)
        first_in, proj_in, tables_in, iota_in, shared_in, sdn_in = [
            act.dma(lambda e, d=dst, s=src: e.dma_start(d, s), dsem(f"const_s{n}"))
            for n, (dst, src) in enumerate(((first_sb[:, :], first), (proj_sb, proj), (tables_sb, tables),
                                            (iota_sb, iota), (shared_sb[:, :], shared), (sdn_sb[:, :, :], sdn)))]

        power = pool(lambda e: e.memset(var, -0.5))
        vones = pool(lambda e: e.memset(v_sb, 1.0))
        kones = [dve(lambda e, i=i: e.memset(ks[i][96:128, :], 1.0)) for i in range(2)]
        huge = [pool(lambda e, v=v: e.memset(v, HUGE)) for v in (sfc, masked, gsum)][-1]
        zero = dve(lambda e: e.memset(zero_sb, 0.0))
        free = [None] * 8
        xnT_ready, xn_read, row_out = [], [None] * NXN, [None] * 4
        row_s = [dsem(f"row_s{i}") for i in range(4)]
        rstd_ready, normalized = [None] * (NT // 2), [None] * (NT // 2)

        def statistics(g):
            for t in (2 * g, 2 * g + 1):
                st = dve(lambda e, t=t: e.bn_stats(stats[:, t, :], xin[:, t, :]), [x_in[g]])
                ag = dve(lambda e, t=t: e.bn_aggr(mv[:, t, :], stats[:, t, :]), [st])
            ve = pool(lambda e: e.tensor_scalar(rstd[:, 2 * g:2 * g + 2], mv[:, 2 * g:2 * g + 2, 1], EPS, None,
                                                ALU.add), [ag])
            rstd_ready[g] = pool(lambda e: e.tensor_tensor(rstd[:, 2 * g:2 * g + 2], rstd[:, 2 * g:2 * g + 2],
                                                           var[:, 2 * g:2 * g + 2], ALU.pow), [ve, power])

        def normalize(g):
            for t in (2 * g, 2 * g + 1):
                s = t % NXN
                nm = dve(lambda e, t=t, s=s: e.tensor_scalar(xn[:, s, :], xin[:, t, :], mv[:, t, 0:1],
                                                             rstd[:, t:t + 1], ALU.subtract, ALU.mult),
                         [rstd_ready[g], xn_read[s], row_out[g % 4]])
                normalized[g] = nm
                b = t % 4 if g < 6 else 6 + t % 2
                for k in range(KC):
                    tr = pe(lambda e, s=s, k=k, b=b: e.transpose(bank[:, b, k * P:(k + 1) * P],
                                                                 xn[:, s, k * P:(k + 1) * P], id_sb),
                            [nm, first_in, free[b]], signal=(k == KC - 1))
                xn_read[s] = tr
                free[b] = act(lambda e, t=t, b=b: e.copy(
                    xnT[:, :, t * P:(t + 1) * P],
                    bank[:, b, 0:D].rearrange("p (a b) -> p a b", a=KC)), [tr])
                xnT_ready.append(free[b])
            if g < 2:
                rows_to_dram(g, act)

        def rows_to_dram(g, queue):
            s = 2 * g % NXN
            row_out[g % 4] = queue.dma(lambda e: e.dma_start(
                rows_d[2 * g * P:(2 * g + 2) * P, 0:D].rearrange("(t p) d -> p t d", p=P),
                xn[:, s:s + 2, :]), row_s[g % 4], [normalized[g]])

        init_s = dsem("init_s")
        w_s = dsem("w_early_s")

        qk_s = [dsem(f"qk_s{i}") for i in range(NPB)]
        stk_s = [dsem(f"stk_s{i}") for i in range(4)]
        stacked = [None] * B
        parts_free, q32_free = [None] * NPB, [None] * NPB
        QP, KP = (0, 0, 1, 1, 0, 2), (0, 1, 0, 1, 2, 0)
        st_read = [None] * B
        wrote_qk = [[] for _ in range(B)]
        proj_unit = [0]
        bias_ready = pool(lambda e: e.tensor_scalar(bq_sb, bq_sb, SCALE, None, ALU.mult), [proj_in])
        vr_ready, vr_read = [None] * B, [None, None]

        def project_steps(b, c, q):
            rows, r0 = (P, 0) if c < KC else (HD, K0)
            for k in range(KC):
                w = wq_sb[:, k, c * P:(c + 1) * P] if c < KC else wvrk_sb[:, k, :]
                mm = pe(lambda e, w=w, k=k: e.matmul(
                    bank[0:r0 + rows, q, :], w, xnT[:, k, b * T:(b + 1) * T], start=(k == 0), stop=(k == KC - 1)),
                    [xnT_ready[4 * b + 3], proj_in, free[q]], signal=(k == KC - 1))
            i = proj_unit[0] % NPB
            subtract = dve if b == 0 or c == KC else pool
            proj_unit[0] += 1
            bias = bq_sb[:, c:c + 1] if c < KC else bk_sb[r0:r0 + rows, 0:1]
            q3, parts3 = q32[r0:r0 + rows, i, :], parts_sb[r0:r0 + rows, i]
            free[q] = q1 = act(lambda e: e.activation(
                q3, bank[r0:r0 + rows, q, :], ACT.Identity, bias=bias, scale=SCALE if c < KC else 1.0),
                [mm, bias_ready, q32_free[i]])
            if c == KC:
                vr_ready[b] = free[q] = act(lambda e: e.copy(vr_sb[0:HD + E, b % 2, :], bank[0:HD + E, q, :]),
                                            [q1, vr_read[b % 2]])
            h1 = act(lambda e: e.copy(parts3[:, 0, :], q3), [q1, parts_free[i]])
            yield
            r1 = subtract(lambda e: e.tensor_tensor(q3, q3, parts3[:, 0, :], ALU.subtract), [h1])
            m1 = act(lambda e: e.copy(parts3[:, 1, :], q3), [r1])
            yield
            q32_free[i] = l1 = subtract(lambda e: e.tensor_tensor(parts3[:, 2, :], q3, parts3[:, 1, :],
                                                                  ALU.subtract), [m1])
            dst = q_d[b, :, c * P:(c + 1) * P, :] if c < KC else k_d[b]
            parts_free[i] = sp.dma(lambda e: e.dma_start(dst.rearrange("a p t -> p a t"), parts3), qk_s[i], [l1])
            wrote_qk[b].append(parts_free[i])

        def project(b, c, q):
            steps = project_steps(b, c, q)
            return [lambda: next(steps, None)] * 3

        def stack(b):
            for r in range(6):
                sp.dma(lambda e, r=r: e.dma_start(
                    qs[b % 2][16 * r:16 * r + 16, :, :],
                    q_d[b, QP[r]].rearrange("(d h) t -> d h t", h=NH)), stk_s[b % 4],
                    wrote_qk[b] + [st_read[b - 2] if b >= 2 else None])
                stacked[b] = sp.dma(lambda e, r=r: e.dma_start(
                    ks[b % 2][16 * r:16 * r + 16, :], k_d[b, KP[r]]), stk_s[b % 4])

        values_ready, scored = [None] * B, [None] * B

        def values_and_logits(b, vb):
            for i in range(IT):
                tr = pe(lambda e, i=i: e.transpose(
                    bank[:, vb, i * (HD + E):(i + 1) * (HD + E)], vr_sb[0:HD + E, b % 2, i * P:(i + 1) * P],
                    id_sb[0:HD + E, 0:HD + E]), [vr_ready[b], free[vb]], signal=(i == IT - 1))
            vr_read[b % 2] = tr
            ts = slice(b * IT, (b + 1) * IT)
            vr = bank[:, vb, 0:IT * (HD + E)].rearrange("p (t c) -> p t c", t=IT)
            values_ready[b] = dve(lambda e: e.tensor_tensor(
                v_sb[:, ts, 0:HD], vr[:, :, 0:HD], bv_sb.unsqueeze(1).to_broadcast([P, IT, HD]), ALU.add),
                [tr, vones])
            free[vb] = scored[b] = act(lambda e: e.activation(scores[:, ts, :], vr[:, :, HD:HD + E], ACT.Sigmoid),
                                       [tr, values_ready[b]])

        tok = {}
        grp = sfc[:, :, 0:E].rearrange("p t (g k) -> p t g k", k=GE)

        def route_groups(n):
            if n == 0:
                tok["gsum"] = dve(lambda e: e.tensor_tensor(
                    sfc[:, :, 0:E], scores, cb_sb.unsqueeze(1).to_broadcast([P, NT, E]), ALU.add), scored + [huge])
            prev = tok["gsum"]
            for a, c in (((0, 1), (0, 2)), ((0, 3), (1, 2)), ((1, 3), (2, 3)))[n]:
                dst = gsum[:, :, 0:G] if (a, c) == (0, 1) else pairs[:, 0]
                prev = dve(lambda e, a=a, c=c, d=dst: e.tensor_tensor(d, grp[:, :, :, a], grp[:, :, :, c], ALU.add),
                           [prev])
                if (a, c) != (0, 1):
                    prev = dve(lambda e: e.tensor_tensor(gsum[:, :, 0:G], gsum[:, :, 0:G], pairs[:, 0], ALU.max),
                               [prev])
            tok["gsum"] = prev

        def route_top(src, dst, key, quarter):
            ts = range(IT * quarter, IT * quarter + IT)
            for t in ts:
                m8 = dve(lambda e, t=t: e.max(top8[:, t, :], src[:, t, :]), [tok[key]])
            for t in ts:
                tok[key + "_top"] = dve(lambda e, t=t: e.match_replace(dst[:, t, :], top8[:, t, :], src[:, t, :], HUGE),
                                        [m8])

        def route_mask():
            g1 = pool(lambda e: e.tensor_scalar(gsel[:, :, 0:G], gsel[:, :, 0:G], HUGE, None, ALU.is_ge),
                     [tok["gsum_top"]])
            g2 = pool(lambda e: e.tensor_scalar(gsel[:, :, 0:G], gsel[:, :, 0:G], -1.0, BIG, ALU.add, ALU.mult), [g1])
            tok["masked"] = pool(lambda e: e.tensor_tensor(
                masked[:, :, 0:E].rearrange("p t (g k) -> p t g k", k=GE), grp,
                gsel[:, :, 0:G].unsqueeze(3).to_broadcast([P, NT, G, GE]), ALU.add), [g2])

        comb_s = dsem("comb_s")

        def route_combine():
            sl = tok["sel"] = pool(lambda e: e.tensor_scalar(sel, picked[:, :, 0:E], HUGE, None, ALU.is_ge),
                                  [tok["masked_top"]])
            tok["selb"] = pool(lambda e: e.tensor_copy(selb, sel), [sl])
            cm = pool(lambda e: e.tensor_tensor(comb, sel, scores, ALU.mult), [sl])
            tok["rows_full"] = sp.dma(lambda e: e.dma_start(
                rows_d[:, D:ROW].rearrange("(t p) e -> p t e", p=P), comb), comb_s, [cm])

        selb2 = selb.rearrange("p t e -> p (t e)")

        def route_totals():
            tot = pe(lambda e: e.matmul(bank[:, 5, :], mask_sb[:, 4, :], selb2, start=True, stop=True),
                     [tok["selb"], masks_ready, free[5]])
            tok["count"] = free[5] = dve(lambda e: e.tensor_reduce(
                cnt, bank[:, 5, :].rearrange("p (t e) -> p e t", e=E), AX, ALU.add), [tot])

        def route_ranks():
            pe(lambda e: e.matmul(bank[:, 4, :], mask_sb[:, 3, :], selb2, start=True, stop=True,
                                  skip_group_check=True), [tok["selb"], masks_ready, free[4]], signal=False)
            for t in range(NT - 1):
                n = NT - 1 - t
                rk = pe(lambda e, t=t, n=n: e.matmul(
                    bank[:, 4, (t + 1) * E:].rearrange("p (t e) -> p t e", e=E), mask_sb[:, 4, :],
                    selb[:, t, :].unsqueeze(1).to_broadcast([P, n, E]), start=False, stop=True,
                    skip_group_check=True), signal=(n == 1))
            tok["rank"] = free[4] = dve(lambda e: e.tensor_copy(
                pos, bank[:, 4, :].rearrange("p (t e) -> p t e", e=E)), [rk])
            ca = cmp_a[:, :, 0:NT]
            c2 = dve(lambda e: e.tensor_tensor(ca, cnt.unsqueeze(2).to_broadcast([P, E, NT]), jc_sb, ALU.is_gt),
                     [tok["count"], tables_in])
            tok["ntile"] = dve(lambda e: e.tensor_reduce(ntile, ca, AX, ALU.add), [c2])

        def route_offsets():
            c4 = pool(lambda e: e.tensor_tensor(cmp_a, ltri_sb, ntile.unsqueeze(1).to_broadcast([P, E, E]), ALU.mult),
                     [tok["ntile"]])
            c5 = dve(lambda e: e.tensor_reduce(offs, cmp_a, AX, ALU.add), [c4])
            c6 = tok["ends"] = pool(lambda e: e.tensor_tensor(ends, offs, ntile, ALU.add), [c5])
            tok["offs"] = pool(lambda e: e.tensor_scalar(offs, offs, float(P), 1.0, ALU.mult, ALU.add), [c6])

        def route_places(n):
            k6 = slice(0, TOPK)
            if n == 0:
                p1 = pool(lambda e: e.tensor_tensor(pos, pos, offs.unsqueeze(1).to_broadcast([P, NT, E]), ALU.add),
                         [tok["rank"], tok["offs"]])
                tok["places"] = pool(lambda e: e.tensor_tensor(pos, pos, sel, ALU.mult), [p1])
            elif n < 5:
                for t in range(IT * (n - 1), IT * n):
                    tok["tops"] = dve(lambda e, t=t: e.max(pos8[:, t, :], pos[:, t, :]), [tok["places"]])
            else:
                p4 = dve(lambda e: e.tensor_scalar(posu[:, :, k6], pos8[:, :, k6], -1.0, None, ALU.add),
                         [tok["tops"]])
                p5 = dve(lambda e: e.tensor_scalar(hiu[:, :, k6], posu[:, :, k6], 7, None,
                                                   ALU.logical_shift_right), [p4])
                p6 = dve(lambda e: e.tensor_scalar(lou[:, :, k6], posu[:, :, k6], P - 1, None, ALU.bitwise_and), [p4])
                dve(lambda e: e.tensor_copy(hi[:, :, k6], hiu[:, :, k6]), [p5])
                tok["places"] = dve(lambda e: e.tensor_copy(lo[:, :, k6], lou[:, :, k6]), [p6])

        def route_slot_experts():
            e1 = dve(lambda e: e.tensor_scalar(ecmp, ends, col_sb[:, 0:1], None, ALU.is_le), [tok["ends"]])
            e2 = dve(lambda e: e.tensor_reduce(ecol[:, 0:1], ecmp, AX, ALU.add), [e1])
            tok["slot_experts"] = dve(lambda e: e.tensor_scalar(ecol[:, 1:2], ecol[:, 0:1], float(E - 1), None,
                                                                ALU.min), [e2])

        def route_experts():
            e4 = pe(lambda e: e.matmul(bank[0:1, 5, 0:P], ecol[:, 1:2], id_sb, start=True, stop=True),
                    [tok["slot_experts"], free[5]])
            tok["experts"] = free[5] = dve(lambda e: e.tensor_copy(erow[:, :], bank[0:1, 5, 0:P]), [e4])

        oh_read = [None]

        def token_numbers():
            for t in range(NT):
                tok["numbers"] = pool(lambda e, t=t: e.tensor_scalar(
                    tokid[:, t:t + 1], col_sb[:, 0:1], float(t * P + 1), None, ALU.add), [first_in])

        def one_hots(b, rows):
            for q in rows:
                t, k = b * IT + q // TOPK, q % TOPK
                eng, key = (dve, "dve_marks") if b > 0 and q % 3 else (pool, "pool_marks")
                tok[key] = eng(lambda e, q=q, t=t, k=k: e.tensor_scalar(
                    oh[:, q, 0, :], iota_sb, hi[:, t, k:k + 1], tokid[:, t:t + 1], ALU.is_equal, ALU.mult),
                    [tok["numbers"], tok["places"], oh_read[0], iota_in])
            tok["row_marks"] = dve(lambda e: e.tensor_tensor(
                oh[:, rows.start:rows.stop, 1, :], iota_sb.unsqueeze(1).to_broadcast([P, len(rows), P]),
                lo[:, t, k - len(rows) + 1:k + 1].unsqueeze(2).to_broadcast([P, len(rows), P]), ALU.is_equal),
                [tok["places"], oh_read[0], iota_in])

        def table_part(b):
            for q in range(NOH):
                mm = pe(lambda e, q=q: e.matmul(bank[:, 7, 0:P], oh[:, q, 1, :], oh[:, q, 0, :],
                                                start=(q == 0), stop=(q == NOH - 1)),
                        [tok["pool_marks"], tok.get("dve_marks"), tok["row_marks"], free[7]], signal=(q == NOH - 1))
            oh_read[0] = mm
            if b == 0:
                free[7] = dve(lambda e: e.tensor_copy(table, bank[:, 7, 0:P]), [mm])
            else:
                free[7] = dve(lambda e: e.tensor_tensor(table, bank[:, 7, 0:P], table, ALU.add), [mm, tok["table"]])
            tok["table"] = free[7]

        S_BANKS, O_BANK, X_BANK = (4, 5), 6, 7
        unit = [0]
        red = [None] * B

        def max_units(b):
            pair = 2 if b == 0 else 1
            units = []
            for i in range(IT):
                nh = (4, 2, 1, 1)[i]
                for h0 in range(0, NH, nh * pair):
                    units.append((i, h0, nh))

            def run(i, h0, nh):
                b0 = 2 * (unit[0] % 3) if b == 0 else S_BANKS[unit[0] % 2]
                unit[0] += 1
                w = (i + 1) * P
                for k in range(pair):
                    for h in range(nh):
                        pe(lambda e, h=h, k=k: e.matmul(
                            bank[:, b0 + k, h * w:(h + 1) * w],
                            qs[b % 2][0:96, h0 + k * nh + h, i * P:(i + 1) * P], ks[b % 2][0:96, 0:w],
                            start=True, stop=True, skip_group_check=True),
                            [stacked[b], free[b0 + k]], signal=False)
                        mm = pe(lambda e, h=h, k=k: e.matmul(
                            bank[:, b0 + k, (h + 1) * w - P:(h + 1) * w], mask_sb[:, 0, :], mask_sb[:, 1, :],
                            start=False, stop=True, skip_group_check=True), [masks_ready],
                            signal=(k == pair - 1 and h == nh - 1))
                red[b] = dve(lambda e: e.tensor_reduce(
                    mx[:, b % 2, h0:h0 + nh * pair, i].rearrange("p (k h) -> p k h", k=pair),
                    bank[:, b0:b0 + pair, 0:nh * w].rearrange("p k (h s) -> p k h s", h=nh), AX, ALU.max),
                    [mm, max_read[b % 2]])
                for k in range(pair):
                    free[b0 + k] = red[b]
            return [lambda a=a: run(*a) for a in units]

        max_s = [dsem(f"max_s{i}") for i in range(2)]
        max_read, mpart_free, max_in = [None, None], [None, None], [None] * B

        def max_clamp(b):
            i = b % 2
            tok["clamped"] = dve(lambda e: e.tensor_scalar(mx[:, i], mx[:, i], -BIG / 10, -1.0, ALU.max, ALU.mult), [red[b]])

        def max_rows(b):
            i = b % 2
            n = NH * IT
            tr = pe(lambda e: e.transpose(bank[0:n, X_BANK, 0:P], mx[:, i].rearrange("p h i -> p (h i)"),
                                          id_sb), [tok["clamped"], free[X_BANK]])
            max_read[i] = tr
            m0 = free[X_BANK] = dve(lambda e: e.tensor_copy(mrow[0:n, 0, :], bank[0:n, X_BANK, 0:P]), [tr])
            h1 = dve(lambda e: e.tensor_copy(mpart[0:n, i, 0, :], mrow[0:n, 0, :]), [m0, mpart_free[i]])
            r1 = dve(lambda e: e.tensor_tensor(mrow[0:n, 1, :], mrow[0:n, 0, :], mpart[0:n, i, 0, :], ALU.subtract), [h1])
            m1 = dve(lambda e: e.tensor_copy(mpart[0:n, i, 1, :], mrow[0:n, 1, :]), [r1])
            l1 = dve(lambda e: e.tensor_tensor(mpart[0:n, i, 2, :], mrow[0:n, 1, :], mpart[0:n, i, 1, :], ALU.subtract), [m1])
            for j in range(3):
                mpart_free[i] = max_in[b] = sp.dma(lambda e, j=j: e.dma_start(
                    qs[i][96 + j:97 + j, :, :].rearrange("p h (i t) -> p (h i) t", t=P),
                    mpart[0:n, i, j, :]), max_s[i], [l1])

        NPX = 4
        p_free = [None] * NPX
        o_free = [None, None]
        att_free = [None]
        pu, su = [0], [0]
        attT_ready = [None] * B

        def attend(b, between):
            i2 = b % 2

            def scores_of(g, j, heads):
                c0, w = j * P, T - j * P
                s2 = su[0] % 2
                su[0] += 1
                px = pu[0] % NPX
                pu[0] += 1
                per = len(heads) // 2
                for k in range(2):
                    sbk = 2 * s2 + k
                    for n in range(per):
                        h = g * ST_GROUP + heads[k * per + n]
                        pe(lambda e, h=h, sbk=sbk, n=n: e.matmul(
                            bank[:, sbk, n * w:(n + 1) * w], ks[i2][0:99, c0:c0 + P], qs[i2][0:99, h, c0:T],
                            start=True, stop=True, skip_group_check=True),
                            [max_in[b], free[2 * s2], free[2 * s2 + 1], kones[i2]], signal=False)
                        mm = pe(lambda e, sbk=sbk, n=n: e.matmul(
                            bank[:, sbk, n * w:n * w + P], mask_sb[:, 0, :], mask_sb[:, 2, :],
                            start=False, stop=True, skip_group_check=True), [masks_ready],
                            signal=(k == 1 and n == per - 1))
                ex = act(lambda e: e.activation(
                    pexp[px][:, :, 0:per * w], bank[:, 2 * s2:2 * s2 + 2, 0:per * w], ACT.Exp),
                    [mm, p_free[px]] + (row_out if b == 0 else []))
                free[2 * s2] = free[2 * s2 + 1] = ex
                return [(px, ex, n // per, n % per * w) for n in range(len(heads))]

            steps = [(g, j) for g in range(NH // ST_GROUP) for j in range(IT)]
            places = 3 * len(steps) - 7
            at = [0, 0]

            def filler():
                at[0] += 1
                upto = min(len(between), -(-len(between) * at[0] // places))
                for f in between[at[1]:upto]:
                    f()
                at[1] = max(at[1], upto)

            late = None
            turned = None
            for g, j in steps:
                at_once = 2 if T - j * P > 256 else 4
                made = scores_of(g, j, range(at_once))
                filler()
                if at_once < ST_GROUP:
                    made += scores_of(g, j, range(at_once, ST_GROUP))
                filler()
                if turned is not None:
                    heads_out(b, *turned)
                    turned = None
                if late is not None:
                    turned = value(b, *late)
                filler()
                late = (g, j, made)
            turned = value(b, *late)
            st_read[b] = made[-1][1]
            heads_out(b, *turned)
            for half in range(2):
                xb = 6 + half
                for i in range(2 * half, 2 * half + 2):
                    for c in range(KC):
                        tr = pe(lambda e, i=i, c=c, xb=xb: e.transpose(
                            bank[:, xb, ((i % 2) * KC + c) * P:((i % 2) * KC + c + 1) * P],
                            att[:, i, c * P:(c + 1) * P], id_sb), [att_done[0], free[xb]])
                free[xb] = act(lambda e, half=half, xb=xb: e.copy(
                    attT[:, :, b * T + half * 2 * P:b * T + (half + 1) * 2 * P].rearrange("p c (i t) -> p i c t", t=P),
                    bank[:, xb, :].rearrange("p (i c t) -> p i c t", i=2, c=KC)), [tr])
            att_free[0] = tr
            attT_ready[b] = free[7]

        att_done = [None]

        def value(b, g, j, made):
            c0, w = j * P, T - j * P
            for k in range(ST_GROUP):
                px, ex, half, o = made[k]
                mm = pe(lambda e, k=k, px=px, half=half, o=o: e.matmul(
                    bank[32 * k:32 * k + 32, O_BANK, c0:T], v_sb[:, b * IT + j, :],
                    pexp[px][:, half, o:o + w], start=(j == 0), stop=True, skip_group_check=True),
                    [ex, values_ready[b], free[O_BANK]], signal=(k == ST_GROUP - 1))
            for px, *_ in made:
                p_free[px] = mm
            if j < IT - 1:
                return None
            s = g % 2
            free[O_BANK] = act(lambda e: e.copy(o_sb[:, s, :], bank[:, O_BANK, :]), [mm, o_free[s]])
            return g, free[O_BANK]

        def heads_out(b, g, copied):
            s = g % 2
            for i in range(IT):
                tr = pe(lambda e, i=i: e.transpose(bank[:, X_BANK, i * P:(i + 1) * P],
                                                   o_sb[:, s, i * P:(i + 1) * P], id_sb),
                        [copied, free[X_BANK]], signal=(i == IT - 1))
            o_free[s] = tr
            o4 = bank[:, X_BANK, :].rearrange("p (i h c) -> p i h c", i=IT, h=ST_GROUP)
            d1 = dve(lambda e: e.tensor_scalar(lrec[:, s], o4[:, :, :, HD], 1.0 / BIG, None, ALU.max), [tr])
            d2 = dve(lambda e: e.reciprocal(lrec[:, s], lrec[:, s]), [d1])
            att_done[0] = free[X_BANK] = dve(lambda e: e.tensor_tensor(
                att[:, :, g * 64:g * 64 + 64].rearrange("p i (h c) -> p i h c", h=ST_GROUP),
                o4[:, :, :, 0:HD], lrec[:, s].unsqueeze(3).to_broadcast([P, IT, ST_GROUP, HD]), ALU.mult),
                [d2, att_free[0]])

        def pieces(*calls):
            return [lambda f=f, args=args: f(*args) for f, *args in calls]

        def table_pieces(b):
            return pieces(*[(one_hots, b, range(q, q + 3)) for q in range(0, NOH, 3)], (table_part, b))

        acc_s = [dsem(f"acc_s{i}") for i in range(NOB)]
        act_free, hidden_ready, down_done, stored = [None, None], {}, [None] * B, [None] * NT
        gu_unit = [0]
        after_routing = []

        def routing_done():
            after_routing.extend([(e.sem, e.count) for e in (pe, act, dve, pool)] + [tok["rows_full"]])

        def gate_up(b, c, pb):
            for up in range(2):
                for k in range(KC):
                    mm = pe(lambda e, up=up, k=k: e.matmul(
                        bank[0:MC, pb + up, :], sgu_sb[:, k, up * 2 * M + c * MC:up * 2 * M + (c + 1) * MC],
                        xnT[:, k, b * T:(b + 1) * T], start=(k == 0), stop=(k == KC - 1)),
                        [free[pb + up], shared_in], signal=(k == KC - 1))
            s = gu_unit[0] % 2
            gu_unit[0] += 1
            n = b * 4 + c
            if b < B - 1:
                h, released = hidden[n % NHB], [down_done[(n - NHB) // 4] if n >= NHB else None]
            else:
                h, released = last_hidden[c], [down_done[(0, 1, 2, 0)[c]]]
            sa = act(lambda e: e.activation(sh_act[:, s, :], bank[0:MC, pb, :], ACT.Silu), [mm, act_free[s]])
            free[pb] = sa
            hm = dve(lambda e: e.tensor_tensor(h[0:MC, :], sh_act[:, s, :], bank[0:MC, pb + 1, :], ALU.mult),
                     [sa] + released + after_routing)
            act_free[s] = free[pb + 1] = hm
            hidden_ready[n] = (h, hm)

        def down(b, i, ob):
            t = b * IT + i
            for c in range(4):
                h, ready = hidden_ready[4 * b + c]
                pe(lambda e, c=c, h=h: e.matmul(
                    bank[:, ob, 0:D], h[0:MC, i * P:(i + 1) * P], sdn_sb[:, c, :],
                    start=(c == 0), stop=False), [ready, free[ob], sdn_in], signal=False)
            for k in range(KC):
                mm = pe(lambda e, k=k: e.matmul(
                    bank[:, ob, 0:D], attT[:, k, t * P:(t + 1) * P], wo_sb[:, k, :],
                    start=False, stop=(k == KC - 1)), [attT_ready[b]], signal=(k == KC - 1))
            if i == IT - 1:
                down_done[b] = mm
            if b < B - 1:
                r, released = ores[t % NOB], [stored[t - NOB] if t >= NOB else None]
            else:
                r, released = last_ores[i], [down_done[B - 2], stored[t - NOB]]
            a1 = free[ob] = dve(lambda e: e.tensor_tensor(r, bank[:, ob, 0:D], bo_sb, ALU.add),
                                [mm, shared_in] + released + after_routing)
            stored[t] = pool.dma(lambda e: e.dma_start(acc_d[0][t * P:(t + 1) * P, :], r), acc_s[t % NOB], [a1])

        def start_accumulators():
            sp.dma(lambda e: e.dma_start(acc_d[1][0:NTOK, :], x), init_s)
            for a in range(2):
                tok["acc_init"] = sp.dma(lambda e, a=a: e.dma_start(acc_d[a][NTOK:NTOK + P, :], zero_sb),
                                         init_s, [zero])

        def early_weights():
            sp.dma(lambda e: e.dma_start(weights[:, 0:EARLY * WCOL], wts[:, 0:EARLY * WCOL]), w_s)

        def merged(a, b):
            out, j = [], 0
            for i, f in enumerate(a):
                out.append(f)
                upto = len(b) * (i + 1) // len(a)
                out += b[j:upto]
                j = upto
            return out

        statistics(0)
        for g in range(2):
            statistics(g + 1)
            normalize(g)
        units = [project_steps(0, c, (6, 7, 4)[c]) for c in (KC, 0, 1)]
        statistics(3)

        def step():
            for u in units:
                next(u, None)
        step()
        normalize(2)
        step()
        normalize(3)
        step()
        stack(0)
        rows_to_dram(2, sp)
        rows_to_dram(3, sp)
        masks_ready = act(lambda e: e.copy(mask_sb, masks32), [tables_in])
        statistics(4)

        def more_rows(g):
            normalize(g)
            rows_to_dram(g, sp)
        statistics(5)
        more_rows(4)
        statistics(6)
        more_rows(5)
        statistics(7)
        values_and_logits(0, 6)
        others = (project(1, KC, 7) + project(1, 0, 6) + pieces((more_rows, 6)) + project(1, 1, 7)
                  + pieces((more_rows, 7), (values_and_logits, 1, 7), (stack, 1)) + project(2, KC, 6)
                  + pieces((values_and_logits, 2, 7)) + project(3, KC, 6) + pieces((values_and_logits, 3, 7)))
        for f in others[:4]:
            f()
        others = others[4:]
        for f in merged(max_units(0), others):
            f()
        act(lambda e: e.activation(lrec[:, 0, 0, 0:1], mv[:, 0, 0:1], ACT.Exp), [scored[B - 1]], signal=False)
        two = [f for both in zip(project(2, 0, 6), project(2, 1, 7)) for f in both]
        max_clamp(0)
        two[0]()
        max_rows(0)
        for f in two[1:]:
            f()
        extra = {
            0: pieces((route_groups, 0), (route_groups, 1), (route_groups, 2), (early_weights,),
                      (start_accumulators,),
                      *[(route_top, gsum, gsel, "gsum", n) for n in range(4)], (route_mask,),
                      *[(route_top, masked, picked, "masked", n) for n in range(4)], (route_combine,)),
            1: pieces((route_totals,)) + project(3, 0, X_BANK) + pieces((route_ranks,), (route_offsets,))
               + project(3, 1, X_BANK) + pieces((route_slot_experts,),
                      *[(route_places, n) for n in range(6)], (route_experts,), (routing_done,), (token_numbers,)),
            2: table_pieces(0),
            3: sum([table_pieces(n)[:-1] + pieces((gate_up, 0, n - 1, 4)) + table_pieces(n)[-1:]
                    for n in (1, 2, 3)], []),
        }
        for b in range(B):
            if b + 1 < B:
                lead = LEAD if b else 0
                between = extra[b][:lead] + merged(max_units(b + 1), extra[b][lead:]) + pieces((max_clamp, b + 1), (max_rows, b + 1))
            else:
                between = extra[b]
            attend(b, between)
            if b + 2 < B:
                stack(b + 2)
        table_ready, rows_full, experts = tok["table"], tok["rows_full"], tok["experts"]
        acc_init = tok["acc_init"]

        t1 = dve(lambda e: e.tensor_scalar(gidx[:, :], table, -1.0, 0.0, ALU.add, ALU.max), [table_ready])
        t2 = dve(lambda e: e.tensor_scalar(tabm[:, 0], table, 0.0, col_sb[:, 1:2], ALU.is_equal, ALU.mult), [t1])
        t3 = dve(lambda e: e.tensor_scalar(tabm[:, 1], table, -1.0, None, ALU.add), [t2])
        indices = dve(lambda e: e.tensor_tensor(sidx[:, :], tabm[:, 0], tabm[:, 1], ALU.add), [t3])

        quiet = [(s.sem, s.count) for s in (pe, act, dve, pool)] + [
            rows_full, acc_init] + parts_free + row_out + mpart_free
        cuts = [MID + (E - MID) * i // PIECES for i in range(PIECES + 1)]
        loaded = [(w_s[0], 16)]
        for i, (e0, e1) in enumerate(zip(cuts, cuts[1:])):
            loaded.append(sp.dma(lambda e, a=e0 * WCOL, b=e1 * WCOL: e.dma_start(weights[:, a:b], wts[:, a:b]),
                                 dsem(f"w_late_s{i}"), quiet if i < 2 else [loaded[i - 1]]))

        AHEAD = 4
        g_s = [dsem(f"g_s{i}") for i in range(NXG)]
        y_s = [dsem(f"y_s{i}") for i in range(NY)]
        gathered, xg_free = [None] * NSLOT, [None] * NXG

        def gather(i):
            s = i % NXG
            gathered[i] = pool.dma(lambda e, i=i, s=s: e.indirect_dma_start(
                out=xg[s], out_offset=None, in_=rows_d[:, :],
                in_offset=bass.IndirectOffsetOnAxis(ap=gidx[:, i:i + 1], axis=0)),
                g_s[s], [xg_free[s], indices, rows_full, xnT_read] + row_out)

        for c in range(3, 4):
            gate_up(0, c, 0)
        for b in range(B):
            if b + 1 < B:
                gate_up(b + 1, 0, 2)
            for i in range(IT):
                down(b, i, 6 + i % 2)
            if b + 1 < B:
                for c in range(1, 4):
                    gate_up(b + 1, c, 2 * ((c + 1) % 2))
            if b == B - 2:
                last_load = sp.dma(lambda e: e.dma_start(
                    weights[:, EARLY * WCOL:MID * WCOL], wts[:, EARLY * WCOL:MID * WCOL]), dsem("w_mid_s"),
                    [down_done[b]] + stored[:(B - 1) * IT])
                loaded.append(last_load)
                xnT_read = (pe.sem, pe.count)
                for i in range(AHEAD):
                    gather(i)
        sh_done = down_done[B - 1]

        regs = {}

        def expert_of(s, i, name, emax=E - 1):
            def load(e, i=i):
                regs[name, i] = e.value_load(erow[0:1, i:i + 1], min_val=0, max_val=emax)
            s.ops.append(([], lambda e, f=load: f(e), None))

        y_free = [None] * NY
        added = [stored + [acc_init], [acc_init]]
        xT_free, sg_free, hh_free, hT_free = [None] * 2, [None] * 2, [None] * 2, [None] * 2
        wflat = weights


        def slot_a(i):
            s, s2 = i % NXG, i % 2
            tb = s2
            for k in range(KC):
                tr = pe(lambda e, k=k: e.transpose(bank[:, tb, k * P:(k + 1) * P], xg[s][:, k * P:(k + 1) * P],
                                                   id_sb), [gathered[i], free[tb]], signal=(k == KC - 1))
            free[tb] = cp = act(lambda e: e.copy(xgT[s2], bank[:, tb, 0:D].rearrange("p (a b) -> p a b", a=KC)),
                                [tr, xT_free[s2], xnT_read])
            return tr, cp

        def slot_b(i, cp):
            s2 = i % 2
            gb = 2 + s2
            expert_of(pe, i, "pe")
            for k in range(KC):
                mm = pe(lambda e, k=k, i=i: e.matmul(
                    bank[:, gb, 0:2 * M], xgT[s2][:, k, :],
                    wflat[:, bass.ds(regs["pe", i] * WCOL + k * 2 * M, 2 * M)],
                    start=(k == 0), stop=(k == KC - 1)), [cp, free[gb]] + loaded + [experts], signal=(k == KC - 1))
            xT_free[s2] = mm
            sa = act(lambda e: e.activation(sg[s2], bank[:, gb, 0:M], ACT.Silu), [mm, sg_free[s2]])
            hm = dve(lambda e: e.tensor_tensor(hh[s2], sg[s2], bank[:, gb, M:2 * M], ALU.mult), [sa, hh_free[s2]])
            sg_free[s2] = free[gb] = hm
            return hm

        def slot_c(i, hm):
            s2 = i % 2
            hb = 4 + s2
            for k in range(2):
                tr = pe(lambda e, k=k: e.transpose(bank[0:MC, hb, k * P:(k + 1) * P],
                                                   hh[s2][:, k * MC:(k + 1) * MC], id_sb),
                        [hm, free[hb]], signal=(k == 1))
            hh_free[s2] = tr
            cp = dve(lambda e: e.tensor_copy(hT[s2][0:MC], bank[0:MC, hb, 0:2 * P].rearrange("p (a b) -> p a b", a=2)),
                     [tr, hT_free[s2]])
            free[hb] = cp
            return cp

        def slot_d(i, cp):
            s, s2, y = i % NXG, i % 2, i % NY
            yb = 6 + s2
            for k in range(2):
                mm = pe(lambda e, k=k, i=i: e.matmul(
                    bank[:, yb, 0:D], hT[s2][0:MC, k, :],
                    wflat[0:MC, bass.ds(regs["pe", i] * WCOL + GU + k * D, D)],
                    start=(k == 0), stop=(k == 1)), [cp, free[yb]], signal=(k == 1))
            hT_free[s2] = mm
            expert_of(dve, i, "dve")
            yw = dve(lambda e, i=i: e.tensor_scalar(ys[y], bank[:, yb, 0:D], xg[s][:, bass.ds(regs["dve", i] + D, 1)],
                                                    None, ALU.mult), [mm, y_free[y], experts, sh_done] + (stored[-IT:] if i < NY else []))
            free[yb] = yw
            xg_free[s] = yw
            a = i % 2 if i < NSLOT - LAST else 0
            y_free[y] = pool.dma(lambda e, i=i: e.indirect_dma_start(
                out=acc_d[a][:, :], out_offset=bass.IndirectOffsetOnAxis(ap=sidx[:, i:i + 1], axis=0),
                in_=ys[y], in_offset=None, compute_op=ALU.add), y_s[y], [yw] + added[a])
            added[a] = [y_free[y]]

        A, Bq, Cq = {}, {}, {}
        for i in range(NSLOT + 3):
            if i + AHEAD < NSLOT:
                gather(i + AHEAD)
            if i < NSLOT:
                A[i] = slot_a(i)[1]
            if 0 <= i - 1 < NSLOT:
                Bq[i - 1] = slot_b(i - 1, A.pop(i - 1))
            if 0 <= i - 3 < NSLOT:
                slot_d(i - 3, Cq.pop(i - 3))
            if 0 <= i - 2 < NSLOT:
                Cq[i - 2] = slot_c(i - 2, Bq.pop(i - 2))

        done, before = [], added[1]
        for h in range(2):
            rows = slice(h * NTOK // 2, (h + 1) * NTOK // 2)
            copied = act.dma(lambda e, r=rows: e.dma_start(out[r, :], acc_d[1][r, :]), dsem(f"copied_s{h}"), before)
            before = [copied]
            done.append(pool.dma(lambda e, r=rows: e.dma_start(
                out[r, :], acc_d[0][r, :], accum_op=ALU.add, max_dma_last_dim=8192), dsem(f"out_s{h}"),
                [copied] + added[0]))
        sp.wait(done)

        block = ctx.enter_context(nc.Block())
        block.sync(sp.play)
        block.scalar(act.play)
        block.vector(dve.play)
        block.gpsimd(pool.play)
        block.tensor(pe.play)


def chunked(a, k):
    return np.ascontiguousarray(a.reshape(k, a.shape[0] // k, -1).transpose(1, 0, 2))


def side_by_side(*parts):
    return np.concatenate([p.reshape(P, -1) for p in parts], 1)


def constants():
    p = np.arange(P)
    ident = np.eye(P, dtype=np.float32)
    masks = np.ones((P, 5, P), np.float32)
    masks[:, 0] = np.eye(P)
    masks[:, 1] = np.where(p[None, :] < p[:, None], 0.0, -BIG)
    masks[:, 2] = masks[:, 1].T
    masks[:, 3] = p[:, None] < p[None, :]
    jc = np.broadcast_to(np.arange(NT, dtype=np.float32) * P, (P, E, NT))
    ltri = np.broadcast_to((np.arange(E)[None, :] < np.arange(E)[:, None]).astype(np.float32), (P, E, E))
    col = np.zeros((P, 4), np.float32)
    col[:, 0] = p
    col[:, 1] = NTOK + 1 + p
    iota = np.broadcast_to(p.astype(np.float16), (P, P))
    return dict(ident=ident, masks=masks, jc=jc, ltri=ltri, col=col, iota=iota)


def kernel(**inputs):
    import concourse.bacc as bacc
    from concourse.bass_utils import run_bass_kernel_spmd

    a = {k.removeprefix("L0_").removeprefix("attn_").removeprefix("ffn_"): np.asarray(v) for k, v in inputs.items()}

    def rows(v):
        return np.broadcast_to(v, (P, v.shape[0]))

    gu = np.stack([a["gate_w"], a["up_w"]], 2).reshape(E, KC, P, 2 * M).transpose(2, 0, 1, 3).reshape(P, E, GU)
    dn = a["down_w"].reshape(E, 2, MC, D).transpose(2, 0, 1, 3).reshape(MC, E, 2 * D)
    dn = np.concatenate([dn, np.zeros((P - MC, E, 2 * D), dn.dtype)], 0)
    wts = np.concatenate([gu, dn], 2).reshape(P, E * WCOL)
    c = constants()
    arrays = dict(
        x=a["q_input"].reshape(NTOK, D),
        first=side_by_side(c["ident"], c["col"]),
        proj=side_by_side(chunked(a["Wq"].reshape(NH, HD, D).transpose(1, 0, 2).reshape(D, D).T, KC),
                          chunked(np.concatenate([a["Wv"].T, a["w_router"],
                                                  np.zeros((D, K0 - HD - E), np.float32), a["Wk"].T], 1), KC),
                          a["bq"].reshape(NH, HD).T.reshape(KC, P).T,
                          np.tile(a["bk"], P // HD), rows(a["bv"]), rows(a["corr_bias"])),
        tables=side_by_side(c["jc"], c["ltri"], c["masks"]), iota=c["iota"],
        shared=side_by_side(rows(a["bo"]), chunked(a["Wo"].T, KC),
                            chunked(np.concatenate([a["sh_gate_w"], a["sh_up_w"]], 1), KC)),
        sdn=chunked(a["sh_down_w"], 4), wts=wts)
    arrays = {f"in_{k}": np.ascontiguousarray(v) for k, v in arrays.items()}
    nc = bacc.Bacc("TRN2", target_bir_lowering=False, num_devices=1)
    args = [nc.dram_tensor(k, v.shape, mybir.dt.from_np(v.dtype), kind="ExternalInput").ap()
            for k, v in arrays.items()]
    y = nc.dram_tensor("out_y", (NTOK, D), F32, kind="ExternalOutput").ap()
    build(nc, *args, y)
    r = run_bass_kernel_spmd(nc, [arrays], core_ids=[0])
    return r.results[0]["out_y"].reshape(B, T, D)
```
